# Optimizing a Trainium2 kernel written in Bass

```python
import numpy as np
import jax
import jax.numpy as jnp

def _softmax(x, axis=-1):
    return jax.nn.softmax(x, axis=axis)

def _gelu(x):
    return jax.nn.gelu(x, approximate=True)

def _silu(x):
    return jax.nn.silu(x)

def _sigmoid(x):
    return jax.nn.sigmoid(x)

def _layernorm(x, axis=-1, eps=1e-05):
    m = jnp.mean(x, axis=axis, keepdims=True)
    v = jnp.var(x, axis=axis, keepdims=True)
    return (x - m) / jnp.sqrt(v + eps)

def _scatter_add(tgt, idx, src, axis=0):
    return tgt.at[idx].add(src)

def _segment_sum(src, seg, n):
    return jax.ops.segment_sum(src, seg, n)
kernel_name = 'mk_dlrm_tower_d1_rec_r8_ae9551'

def setup_inputs(seed: int=0):
    np.random.seed(seed)
    _w = jnp.asarray

    def _rec_inputs():
        import jax
        import jax.numpy as jnp
        _tk = jax.random.key(seed)
        dense_ctx = jax.random.normal(jax.random.fold_in(_tk, 190), (2048, 16), jnp.float32)
        ids = jnp.stack([jax.random.randint(jax.random.fold_in(_tk, 200 + f), (2048,), 0, v, jnp.int32) for f, v in enumerate([12500, 1000, 1250, 12500, 1250, 1250, 1000, 12500, 12500, 1250, 1250, 1250, 1250, 1250, 1250, 1250, 1250, 12500, 1000, 1250, 12500, 12500, 1250, 1000, 1000, 1000, 1250, 1250, 1000, 1250, 1250, 1000])], axis=1)
        tbl_0 = 0.05 * jax.random.normal(jax.random.fold_in(_tk, 500 + 0), (12500, 256), jnp.float32)
        tbl_1 = 0.05 * jax.random.normal(jax.random.fold_in(_tk, 500 + 1), (1000, 256), jnp.float32)
        tbl_2 = 0.05 * jax.random.normal(jax.random.fold_in(_tk, 500 + 2), (1250, 256), jnp.float32)
        tbl_3 = 0.05 * jax.random.normal(jax.random.fold_in(_tk, 500 + 3), (12500, 256), jnp.float32)
        tbl_4 = 0.05 * jax.random.normal(jax.random.fold_in(_tk, 500 + 4), (1250, 256), jnp.float32)
        tbl_5 = 0.05 * jax.random.normal(jax.random.fold_in(_tk, 500 + 5), (1250, 256), jnp.float32)
        tbl_6 = 0.05 * jax.random.normal(jax.random.fold_in(_tk, 500 + 6), (1000, 256), jnp.float32)
        tbl_7 = 0.05 * jax.random.normal(jax.random.fold_in(_tk, 500 + 7), (12500, 256), jnp.float32)
        tbl_8 = 0.05 * jax.random.normal(jax.random.fold_in(_tk, 500 + 8), (12500, 256), jnp.float32)
        tbl_9 = 0.05 * jax.random.normal(jax.random.fold_in(_tk, 500 + 9), (1250, 256), jnp.float32)
        tbl_10 = 0.05 * jax.random.normal(jax.random.fold_in(_tk, 500 + 10), (1250, 256), jnp.float32)
        tbl_11 = 0.05 * jax.random.normal(jax.random.fold_in(_tk, 500 + 11), (1250, 256), jnp.float32)
        tbl_12 = 0.05 * jax.random.normal(jax.random.fold_in(_tk, 500 + 12), (1250, 256), jnp.float32)
        tbl_13 = 0.05 * jax.random.normal(jax.random.fold_in(_tk, 500 + 13), (1250, 256), jnp.float32)
        tbl_14 = 0.05 * jax.random.normal(jax.random.fold_in(_tk, 500 + 14), (1250, 256), jnp.float32)
        tbl_15 = 0.05 * jax.random.normal(jax.random.fold_in(_tk, 500 + 15), (1250, 256), jnp.float32)
        tbl_16 = 0.05 * jax.random.normal(jax.random.fold_in(_tk, 500 + 16), (1250, 256), jnp.float32)
        tbl_17 = 0.05 * jax.random.normal(jax.random.fold_in(_tk, 500 + 17), (12500, 256), jnp.float32)
        tbl_18 = 0.05 * jax.random.normal(jax.random.fold_in(_tk, 500 + 18), (1000, 256), jnp.float32)
        tbl_19 = 0.05 * jax.random.normal(jax.random.fold_in(_tk, 500 + 19), (1250, 256), jnp.float32)
        tbl_20 = 0.05 * jax.random.normal(jax.random.fold_in(_tk, 500 + 20), (12500, 256), jnp.float32)
        tbl_21 = 0.05 * jax.random.normal(jax.random.fold_in(_tk, 500 + 21), (12500, 256), jnp.float32)
        tbl_22 = 0.05 * jax.random.normal(jax.random.fold_in(_tk, 500 + 22), (1250, 256), jnp.float32)
        tbl_23 = 0.05 * jax.random.normal(jax.random.fold_in(_tk, 500 + 23), (1000, 256), jnp.float32)
        tbl_24 = 0.05 * jax.random.normal(jax.random.fold_in(_tk, 500 + 24), (1000, 256), jnp.float32)
        tbl_25 = 0.05 * jax.random.normal(jax.random.fold_in(_tk, 500 + 25), (1000, 256), jnp.float32)
        tbl_26 = 0.05 * jax.random.normal(jax.random.fold_in(_tk, 500 + 26), (1250, 256), jnp.float32)
        tbl_27 = 0.05 * jax.random.normal(jax.random.fold_in(_tk, 500 + 27), (1250, 256), jnp.float32)
        tbl_28 = 0.05 * jax.random.normal(jax.random.fold_in(_tk, 500 + 28), (1000, 256), jnp.float32)
        tbl_29 = 0.05 * jax.random.normal(jax.random.fold_in(_tk, 500 + 29), (1250, 256), jnp.float32)
        tbl_30 = 0.05 * jax.random.normal(jax.random.fold_in(_tk, 500 + 30), (1250, 256), jnp.float32)
        tbl_31 = 0.05 * jax.random.normal(jax.random.fold_in(_tk, 500 + 31), (1000, 256), jnp.float32)
        _rk = jax.random.fold_in(_tk, 7)
        W_top1 = 0.0441942 * jax.random.normal(jax.random.fold_in(_tk, 801), (512, 512), jnp.float32)
        W_top2 = 0.0441942 * jax.random.normal(jax.random.fold_in(_tk, 802), (512, 256), jnp.float32)
        W_top3 = 0.0625 * jax.random.normal(jax.random.fold_in(_tk, 803), (256, 1), jnp.float32)
        b_top1 = jnp.zeros((512,), jnp.float32)
        b_top2 = jnp.zeros((256,), jnp.float32)
        return (dense_ctx, ids, tbl_0, tbl_1, tbl_2, tbl_3, tbl_4, tbl_5, tbl_6, tbl_7, tbl_8, tbl_9, tbl_10, tbl_11, tbl_12, tbl_13, tbl_14, tbl_15, tbl_16, tbl_17, tbl_18, tbl_19, tbl_20, tbl_21, tbl_22, tbl_23, tbl_24, tbl_25, tbl_26, tbl_27, tbl_28, tbl_29, tbl_30, tbl_31, W_top1, b_top1, W_top2, b_top2, W_top3)
    dense_ctx, ids, tbl_0, tbl_1, tbl_2, tbl_3, tbl_4, tbl_5, tbl_6, tbl_7, tbl_8, tbl_9, tbl_10, tbl_11, tbl_12, tbl_13, tbl_14, tbl_15, tbl_16, tbl_17, tbl_18, tbl_19, tbl_20, tbl_21, tbl_22, tbl_23, tbl_24, tbl_25, tbl_26, tbl_27, tbl_28, tbl_29, tbl_30, tbl_31, W_top1, b_top1, W_top2, b_top2, W_top3 = _rec_inputs()

    def _L0_rec_setup():
        import jax, jax.numpy as jnp
        import numpy as np
        B, N, D = (1024, 32, 256)
        key = jax.random.key(seed)
        x = jax.random.normal(key, (B, N, D), dtype=jnp.float32)
        return {'x': x}
    _L0_rec_all = _L0_rec_setup()
    _L0_rec_in = {k: v for k, v in _L0_rec_all.items() if k in ()}
    del _L0_rec_all
    return {'dense_ctx': dense_ctx, 'ids': ids, 'tbl_0': tbl_0, 'tbl_1': tbl_1, 'tbl_2': tbl_2, 'tbl_3': tbl_3, 'tbl_4': tbl_4, 'tbl_5': tbl_5, 'tbl_6': tbl_6, 'tbl_7': tbl_7, 'tbl_8': tbl_8, 'tbl_9': tbl_9, 'tbl_10': tbl_10, 'tbl_11': tbl_11, 'tbl_12': tbl_12, 'tbl_13': tbl_13, 'tbl_14': tbl_14, 'tbl_15': tbl_15, 'tbl_16': tbl_16, 'tbl_17': tbl_17, 'tbl_18': tbl_18, 'tbl_19': tbl_19, 'tbl_20': tbl_20, 'tbl_21': tbl_21, 'tbl_22': tbl_22, 'tbl_23': tbl_23, 'tbl_24': tbl_24, 'tbl_25': tbl_25, 'tbl_26': tbl_26, 'tbl_27': tbl_27, 'tbl_28': tbl_28, 'tbl_29': tbl_29, 'tbl_30': tbl_30, 'tbl_31': tbl_31, 'W_top1': W_top1, 'b_top1': b_top1, 'W_top2': W_top2, 'b_top2': b_top2, 'W_top3': W_top3}

def reference(dense_ctx, ids, tbl_0, tbl_1, tbl_2, tbl_3, tbl_4, tbl_5, tbl_6, tbl_7, tbl_8, tbl_9, tbl_10, tbl_11, tbl_12, tbl_13, tbl_14, tbl_15, tbl_16, tbl_17, tbl_18, tbl_19, tbl_20, tbl_21, tbl_22, tbl_23, tbl_24, tbl_25, tbl_26, tbl_27, tbl_28, tbl_29, tbl_30, tbl_31, W_top1, b_top1, W_top2, b_top2, W_top3):
    import jax
    import jax.numpy as jnp

    def _L0_rec_ref(x):
        import jax, jax.numpy as jnp
        import numpy as np
        B, N, D = (1024, 32, 256)
        'Second-order feature interaction (DLRM dot interaction).\n\n            Computes dot(x_i, x_j) for all field pairs i < j (self_interaction=False),\n            flattened in row-major upper-triangular order -> [B, N*(N-1)/2].\n            Matches tf.boolean_mask(dot_products, strictly_upper_mask) ordering.\n            '
        b, n, d = x.shape
        iu, ju = jnp.triu_indices(n, k=1)
        dots = jnp.einsum('bnd,bmd->bnm', x, x)
        return dots[:, iu, ju]
    e = jnp.stack([tbl_0[ids[:, 0]], tbl_1[ids[:, 1]], tbl_2[ids[:, 2]], tbl_3[ids[:, 3]], tbl_4[ids[:, 4]], tbl_5[ids[:, 5]], tbl_6[ids[:, 6]], tbl_7[ids[:, 7]], tbl_8[ids[:, 8]], tbl_9[ids[:, 9]], tbl_10[ids[:, 10]], tbl_11[ids[:, 11]], tbl_12[ids[:, 12]], tbl_13[ids[:, 13]], tbl_14[ids[:, 14]], tbl_15[ids[:, 15]], tbl_16[ids[:, 16]], tbl_17[ids[:, 17]], tbl_18[ids[:, 18]], tbl_19[ids[:, 19]], tbl_20[ids[:, 20]], tbl_21[ids[:, 21]], tbl_22[ids[:, 22]], tbl_23[ids[:, 23]], tbl_24[ids[:, 24]], tbl_25[ids[:, 25]], tbl_26[ids[:, 26]], tbl_27[ids[:, 27]], tbl_28[ids[:, 28]], tbl_29[ids[:, 29]], tbl_30[ids[:, 30]], tbl_31[ids[:, 31]]], axis=1)
    z = _L0_rec_ref(e)
    z = z.reshape(z.shape[0], -1)
    h = jnp.concatenate([z, dense_ctx], axis=1)
    h = jnp.maximum(h @ W_top1 + b_top1, 0.0)
    h = jnp.maximum(h @ W_top2 + b_top2, 0.0)
    y = h @ W_top3
    return y

_drawn_inputs = setup_inputs


def setup_inputs(seed=0):
    import zlib

    import numpy as np

    out = dict(_drawn_inputs(seed))
    spreads = {'b_top1': (0.0, 0.1), 'b_top2': (0.0, 0.1)}
    factors = {}
    for name, (base, spread) in spreads.items():
        noise = np.random.default_rng([zlib.crc32(name.encode()), seed]).standard_normal(out[name].shape)
        drawn = base * np.exp(spread * noise) if base else spread * noise
        out[name] = jnp.asarray(drawn.astype(out[name].dtype))
    for name, factor in factors.items():
        out[name] = (out[name] * factor).astype(out[name].dtype)
    return out
```

```python
from contextlib import ExitStack

import concourse.bass as bass
from concourse import mybir

P = 128
F32 = mybir.dt.float32
U32 = mybir.dt.uint32
ALU = mybir.AluOpType
ACT = mybir.ActivationFunctionType

N_FEAT = 32
DEPTH = 256
HALVES = DEPTH // P
N_DENSE = 16
QUADS = P // 4
GROUP = 8
GROUPS = QUADS // GROUP
PAIRS = N_FEAT // 2
SLOTS = 8
K_TILES = 5
LATE = 24 * 16
CORNERS = LATE + 8 * 16
CORNER = 8 * 8


def pair_rows():
    def row(m, i):
        return i * (2 * N_FEAT - i - 1) // 2 + (m - i - 1) if i < m else -1

    rows = [row(m, i) for m in range(8, 32) for i in range(16)]
    rows += [row(m, i) for m in range(24, 32) for i in range(16, 32)]
    for corner in (0, 16):
        rows += [row(corner + m, corner + i) for m in range(8) for i in range(8)]
    n_pairs = N_FEAT * (N_FEAT - 1) // 2
    for c in range(N_DENSE):
        rows[CORNERS + CORNER * (c // 8) + c % 8] = n_pairs + c
    assert sorted(r for r in rows if r >= 0) == list(range(n_pairs + N_DENSE))
    return rows


def build(nc, ids, dense, tables, w1, b1, w2, b2, w3, y):
    batch = dense.shape[0]
    TILES = batch // P
    H1, H2 = w1.shape[2], w2.shape[1]
    M1, M2 = H1 // P, H2 // P

    with ExitStack() as ctx:
        def sb(name, shape, dt=F32):
            return ctx.enter_context(nc.sbuf_tensor(name, shape, dt))

        def ps(name, shape):
            return ctx.enter_context(nc.psum_tensor(name, shape, F32))

        def sem(name):
            return ctx.enter_context(nc.semaphore(name))

        ids_sb = [sb(f"ids_sb{k}", [P, N_FEAT], U32) for k in range(2)]
        X = sb("X", [P, N_FEAT, DEPTH])
        XT = [sb(f"XT{k}", [P, HALVES, P, N_FEAT]) for k in range(2)]
        Z = sb("Z", [P, N_FEAT, QUADS])
        T = sb("T", [P, N_FEAT, N_FEAT])
        C = sb("C", [P, K_TILES * P])
        TT = sb("TT", [P, K_TILES, P])
        h1 = sb("h1", [P, M1, P])
        h2 = sb("h2", [P, M2, P])
        y_sb = sb("y_sb", [1, batch])
        dense_sb = sb("dense_sb", [P, TILES, N_DENSE])
        w1_sb = sb("w1_sb", [P, K_TILES, H1])
        w2_sb = sb("w2_sb", [P, M1, H2])
        w3_sb = sb("w3_sb", [P, M2])
        b1_sb = sb("b1_sb", [P, M1])
        b2_sb = sb("b2_sb", [P, M2])
        ident = sb("ident", [P, P])

        xt_ps = [ps(f"xt_ps{k}", [P, 2, HALVES, P]) for k in range(2)]
        dots_ps = [ps(f"dots_ps{k}", [P, GROUP, P]) for k in range(2)]
        bank_a = ps("bank_a", [P, 4, P])
        bank_b = ps("bank_b", [P, 4, P])
        banks = [bank_a, bank_b]

        ids_landed = [sem(f"ids_landed{k}") for k in range(2)]
        gathered = [sem(f"gathered{f}") for f in range(N_FEAT)]
        dense_landed = sem("dense_landed")
        w1_landed = sem("w1_landed")
        w2_landed = sem("w2_landed")
        small_landed = sem("small_landed")
        ident_zeroed = sem("ident_zeroed")
        ident_ready = sem("ident_ready")
        ids_waited = sem("ids_waited")
        slots_waited = sem("slots_waited")
        turned = sem("turned")
        xt_by_dve = sem("xt_by_dve")
        xt_by_act = sem("xt_by_act")
        dots_done = sem("dots_done")
        z_by_dve = sem("z_by_dve")
        z_by_act = sem("z_by_act")
        z_turned = sem("z_turned")
        c_by_act = sem("c_by_act")
        c_turned = sem("c_turned")
        tt_by_dve = sem("tt_by_dve")
        tt_by_act = sem("tt_by_act")
        h1_summed = sem("h1_summed")
        h1_ready = sem("h1_ready")
        h2_summed = sem("h2_summed")
        h2_ready = sem("h2_ready")
        y_summed = sem("y_summed")
        y_ready = sem("y_ready")
        y_stored = sem("y_stored")

        y_q = y_sb[:, :].rearrange("o (t q j) -> o t j q", q=QUADS, j=4)
        ids_tiles = ids.bitcast(U32).rearrange("(t p) f -> t p f", p=P)

        block = ctx.enter_context(nc.Block())

        @block.sync
        def _(sp):
            def load_ids(t, k):
                sp.dma_start(ids_sb[k][:, :], ids_tiles[t]).then_inc(ids_landed[k], 16)

            load_ids(0, 0)
            load_ids(1, 1)
            dense_q = dense.rearrange("(t q j) c -> j q t c", j=4, q=QUADS)
            for j in range(4):
                sp.dma_start(dense_sb[32 * j:32 * j + 32, :, :], dense_q[j]).then_inc(dense_landed, 16)
            sp.dma_start(w1_sb[:, :, :], w1.rearrange("k p n -> p k n")).then_inc(w1_landed, 16)
            sp.dma_start(w2_sb[:, :, :], w2.rearrange("(k p) n -> p k n", p=P)).then_inc(w2_landed, 16)
            sp.dma_start(b1_sb[:, :], b1).then_inc(small_landed, 16)
            sp.dma_start(b2_sb[:, :], b2).then_inc(small_landed, 16)
            sp.dma_start(w3_sb[:, :], w3).then_inc(small_landed, 16)
            with sp.Fori(1, TILES // 2) as i:
                for k in range(2):
                    sp.wait_ge(turned, PAIRS * (2 * i + k - 1))
                    sp.dma_start(ids_sb[k][:, :], ids_tiles[2 * i + k]).then_inc(ids_landed[k], 16)
            sp.wait_ge(y_ready, TILES)
            sp.dma_start(y.rearrange("b o -> o b"), y_sb[:, :]).then_inc(y_stored, 16)
            sp.wait_ge(y_stored, 16)

        @block.gpsimd
        def _(pool):
            def gather_tile(t, k, first=False):
                pool.wait_ge(ids_landed[k], 8 * (t - k) + 16)
                pool.sem_inc(ids_waited, 1)
                for f in range(N_FEAT):
                    if not first and f % SLOTS == 0:
                        pool.wait_ge(turned, PAIRS * (t - 1) + (f + SLOTS) // 2)
                        pool.sem_inc(slots_waited, 1)
                    pool.indirect_dma_start(
                        X[:, f, :], None, tables[f], bass.IndirectOffsetOnAxis(ids_sb[k][:, f:f + 1], 0)
                    ).then_inc(gathered[f], 16)

            gather_tile(0, 0, first=True)
            pool.memset(ident[:, :], 0.0).then_inc(ident_zeroed, 1)
            pool.wait_ge(ident_zeroed, 1)
            pool.affine_select(out=ident[:, :], in_=ident[:, :], compare_op=ALU.not_equal, fill=1.0,
                               base=0, pattern=[[-1, P]], channel_multiplier=1).then_inc(ident_ready, 1)
            with pool.Fori(1, TILES // 2) as i:
                gather_tile(2 * i - 1, 1)
                gather_tile(2 * i, 0)
            gather_tile(TILES - 1, 1)

        @block.tensor
        def _(pe):
            def turn_pair(t, pair, first=False):
                if not (first and pair < 2):
                    pe.wait_ge((xt_by_dve, xt_by_act)[pair % 2], PAIRS // 2 * t + pair // 2)
                for e in range(2):
                    f = 2 * pair + e
                    pe.wait_ge(gathered[f], 16 * (t + 1))
                    for h in range(HALVES):
                        last = pe.transpose(xt_ps[pair % 2][:, e, h, :], X[:, f, h * P:(h + 1) * P], ident[:, :])
                last.then_inc(turned, 1)

            def dots_of(u, k, quad, first=False):
                if quad == 0:
                    pe.wait_ge(xt_by_dve, PAIRS // 2 * (u + 1))
                    pe.wait_ge(xt_by_act, PAIRS // 2 * (u + 1))
                g = quad // GROUP
                if quad % GROUP == 0 and not (first and g < 2):
                    pe.wait_ge(z_by_dve, GROUPS * u + g - 1)
                    pe.wait_ge(z_by_act, GROUPS * u + g - 1)
                for h in range(HALVES):
                    rows = XT[k][:, h, 4 * quad:4 * quad + 4, :].rearrange("p j f -> p (j f)")
                    last = pe.matmul(dots_ps[g % 2][:, quad % GROUP, :], rows, rows,
                                     start=(h == 0), stop=(h == HALVES - 1))
                if quad % GROUP == GROUP - 1:
                    last.then_inc(dots_done, 1)

            def layers(u, first=False):
                pe.wait_ge(c_by_act, u + 1)
                if not first:
                    pe.wait_ge(y_ready, u)
                for n in range(K_TILES):
                    out = bank_a[:, n, :] if n < 4 else bank_b[:, 0, :]
                    last = pe.transpose(out, C[:, n * P:(n + 1) * P], ident[:, :])
                last.then_inc(c_turned, 1)

                if first:
                    pe.wait_ge(w1_landed, 16)
                pe.wait_ge(tt_by_dve, u + 1)
                pe.wait_ge(tt_by_act, u + 1)
                for m in range(M1):
                    if m >= 2:
                        pe.wait_ge(h1_ready, M1 * u + m - 1)
                    for k in range(K_TILES):
                        last = pe.matmul(banks[m % 2][:, m, :], w1_sb[:, k, m * P:(m + 1) * P], TT[:, k, :],
                                         start=(k == 0), stop=(k == K_TILES - 1))
                    last.then_inc(h1_summed, 1)
                if first:
                    pe.wait_ge(w2_landed, 16)
                pe.wait_ge(h1_ready, M1 * (u + 1))
                for m in range(M2):
                    for k in range(M1):
                        last = pe.matmul(banks[m % 2][:, m, :], w2_sb[:, k, m * P:(m + 1) * P], h1[:, k, :],
                                         start=(k == 0), stop=(k == M1 - 1))
                    last.then_inc(h2_summed, 1)
                if first:
                    pe.wait_ge(small_landed, 48)
                pe.wait_ge(h2_ready, M2 * (u + 1))
                for k in range(M2):
                    last = pe.matmul(bank_a[0:1, 3, :], w3_sb[:, k:k + 1], h2[:, k, :],
                                     start=(k == 0), stop=(k == M2 - 1))
                last.then_inc(y_summed, 1)

            def tile_step(t, k, first=False):
                for pair in range(PAIRS):
                    turn_pair(t, pair)
                    dots_of(t - 1, k, 2 * pair, first)
                    dots_of(t - 1, k, 2 * pair + 1, first)
                layers(t - 1, first)

            pe.wait_ge(ident_ready, 1)
            for pair in range(PAIRS):
                turn_pair(0, pair, first=True)
            tile_step(1, 0, first=True)
            with pe.Fori(1, TILES // 2) as i:
                tile_step(2 * i, 1)
                tile_step(2 * i + 1, 0)
            for quad in range(QUADS):
                dots_of(TILES - 1, 1, quad)
            layers(TILES - 1)

        def copy_dots(engine_copy, g, j):
            lanes = slice(32 * j, 32 * j + 32)
            src = dots_ps[g % 2][lanes, :, 32 * j:32 * j + 32]
            dst = Z[lanes, :, g * GROUP:(g + 1) * GROUP].rearrange("p m q -> p q m")
            return engine_copy(dst, src)

        def copy_turned(engine_copy, k, pair):
            dst = XT[k][:, :, :, 2 * pair:2 * pair + 2].rearrange("p h b e -> p e h b")
            return engine_copy(dst, xt_ps[pair % 2][:, :, :, :])

        @block.vector
        def _(dve):
            def copy(dst, src):
                return dve.tensor_copy(dst, src)

            def even_pair(t, k, pair, early=False):
                dve.wait_ge(turned, PAIRS * t + pair + 1)
                if pair == 0 and not early:
                    dve.wait_ge(dots_done, GROUPS * (t - 1))
                copy_turned(copy, k, pair).then_inc(xt_by_dve, 1)

            def dots_group(u, g):
                dve.wait_ge(dots_done, GROUPS * u + g + 1)
                copy_dots(copy, g, 0)
                copy_dots(copy, g, 1).then_inc(z_by_dve, 1)

            def operand(u, first=False):
                dve.wait_ge(z_by_dve, GROUPS * (u + 1))
                dve.wait_ge(z_by_act, GROUPS * (u + 1))
                if not first:
                    dve.wait_ge(c_by_act, u)
                dve.transpose(T[:, :, :], Z[:, :, :]).then_inc(z_turned, 1)
                dve.wait_ge(c_turned, u + 1)
                dve.tensor_copy(TT[:, 0:4, :], bank_a[:, :, :]).then_inc(tt_by_dve, 1)

            def tile_step(t, k, early=False):
                for pair in range(0, PAIRS, 2):
                    even_pair(t, k, pair, early)
                    if pair % 4 == 2:
                        dots_group(t - 1, pair // 4)
                operand(t - 1, early)

            for pair in range(0, PAIRS, 2):
                even_pair(0, 0, pair, early=True)
            tile_step(1, 1, early=True)
            with dve.Fori(1, TILES // 2) as i:
                tile_step(2 * i, 0)
                tile_step(2 * i + 1, 1)
            for g in range(GROUPS):
                dots_group(TILES - 1, g)
            operand(TILES - 1)

        @block.scalar
        def _(act):
            def copy(dst, src):
                return act.activation(dst, src, ACT.Copy)

            def odd_pair(t, k, pair, early=False):
                act.wait_ge(turned, PAIRS * t + pair + 1)
                if pair == 1 and not early:
                    act.wait_ge(dots_done, GROUPS * (t - 1))
                copy_turned(copy, k, pair).then_inc(xt_by_act, 1)

            def dots_group(u, g, first=False):
                act.wait_ge(dots_done, GROUPS * u + g + 1)
                if g == 0 and not first:
                    act.wait_ge(z_turned, u)
                copy_dots(copy, g, 2)
                copy_dots(copy, g, 3).then_inc(z_by_act, 1)

            def layers(u, first=False):
                corners = C[:, CORNERS:].rearrange("p (a m i) -> p a m i", a=2, i=8)
                if first:
                    act.wait_ge(dense_landed, 64)
                else:
                    act.wait_ge(c_turned, u)
                copy(corners[:, :, 0, :], dense_sb[:, u, :].rearrange("p (a c) -> p a c", a=2))
                act.wait_ge(z_turned, u + 1)
                copy(C[:, 0:LATE].rearrange("p (m i) -> p m i", i=16), T[:, 8:32, 0:16])
                copy(C[:, LATE:CORNERS].rearrange("p (m i) -> p m i", i=16), T[:, 24:32, 16:32])
                copy(corners[:, 0, 1:8, :], T[:, 1:8, 0:8])
                copy(corners[:, 1, 1:8, :], T[:, 17:24, 16:24]).then_inc(c_by_act, 1)
                act.wait_ge(c_turned, u + 1)
                copy(TT[:, 4, :], bank_b[:, 0, :]).then_inc(tt_by_act, 1)
                if first:
                    act.wait_ge(small_landed, 48)
                for m in range(M1):
                    act.wait_ge(h1_summed, M1 * u + m + 1)
                    act.activation(h1[:, m, :], banks[m % 2][:, m, :], ACT.Relu, bias=b1_sb[:, m:m + 1]).then_inc(h1_ready, 1)
                for m in range(M2):
                    act.wait_ge(h2_summed, M2 * u + m + 1)
                    act.activation(h2[:, m, :], banks[m % 2][:, m, :], ACT.Relu, bias=b2_sb[:, m:m + 1]).then_inc(h2_ready, 1)
                act.wait_ge(y_summed, u + 1)
                copy(y_q[:, u, :, :], bank_a[0:1, 3, :].rearrange("o (j q) -> o j q", j=4)).then_inc(y_ready, 1)

            def tile_step(t, k, first=False):
                for pair in range(1, PAIRS, 2):
                    odd_pair(t, k, pair, first)
                    if pair % 4 == 3:
                        dots_group(t - 1, pair // 4, first)
                layers(t - 1, first)

            for pair in range(1, PAIRS, 2):
                odd_pair(0, 0, pair, early=True)
            tile_step(1, 1, first=True)
            with act.Fori(1, TILES // 2) as i:
                tile_step(2 * i, 0)
                tile_step(2 * i + 1, 1)
            for g in range(GROUPS):
                dots_group(TILES - 1, g)
            layers(TILES - 1)


def kernel(**inputs):
    import numpy as np
    import concourse.bacc as bacc
    from concourse.bass_utils import run_bass_kernel_spmd

    nc = bacc.Bacc("TRN2", target_bir_lowering=False, num_devices=1)
    arrays = {}

    def given(name, a):
        a = np.ascontiguousarray(a)
        arrays[name] = a
        return nc.dram_tensor(name, a.shape, mybir.dt.from_np(a.dtype), kind="ExternalInput").ap()

    w_top1 = np.asarray(inputs["W_top1"])
    w1 = np.zeros((K_TILES * P, w_top1.shape[1]), w_top1.dtype)
    rows = np.array(pair_rows())
    w1[rows >= 0] = w_top1[rows[rows >= 0]]

    ids = given("ids", inputs["ids"])
    dense = given("dense_ctx", inputs["dense_ctx"])
    tables = [given(f"tbl_{f}", inputs[f"tbl_{f}"]) for f in range(N_FEAT)]
    w1 = given("w1", w1.reshape(K_TILES, P, -1))
    b1 = given("b1", np.asarray(inputs["b_top1"]).reshape(-1, P).T)
    w2 = given("w2", inputs["W_top2"])
    b2 = given("b2", np.asarray(inputs["b_top2"]).reshape(-1, P).T)
    w3 = given("w3", np.asarray(inputs["W_top3"]).reshape(-1, P).T)
    y = nc.dram_tensor("y", (dense.shape[0], 1), F32, kind="ExternalOutput").ap()
    build(nc, ids, dense, tables, w1, b1, w2, b2, w3, y)
    result = run_bass_kernel_spmd(nc, [arrays], core_ids=[0])
    return result.results[0]["y"]
```

```python
from contextlib import ExitStack

import concourse.bass as bass
from concourse import mybir

P = 128
F32 = mybir.dt.float32
F32R = mybir.dt.float32r
U32 = mybir.dt.uint32
ALU = mybir.AluOpType
ACT = mybir.ActivationFunctionType

N_FEAT = 32
DEPTH = 256
HALVES = DEPTH // P
N_DENSE = 16
QUADS = P // 4
GROUP = 4
GROUPS = QUADS // GROUP
PAIRS = N_FEAT // 2
SLOTS = 8
LOOKED = (1, 6, 18)
N_LOOK = len(LOOKED)
ROW_TILES = 8
K_TILES = 5
LATE = 24 * 16
CORNERS = LATE + 8 * 16
CORNER = 8 * 8


def pair_rows():
    def row(m, i):
        return i * (2 * N_FEAT - i - 1) // 2 + (m - i - 1) if i < m else -1

    rows = [row(m, i) for m in range(8, 32) for i in range(16)]
    rows += [row(m, i) for m in range(24, 32) for i in range(16, 32)]
    for corner in (0, 16):
        rows += [row(corner + m, corner + i) for m in range(8) for i in range(8)]
    n_pairs = N_FEAT * (N_FEAT - 1) // 2
    for c in range(N_DENSE):
        rows[CORNERS + CORNER * (c // 8) + c % 8] = n_pairs + c
    assert sorted(r for r in rows if r >= 0) == list(range(n_pairs + N_DENSE))
    return rows


def build(nc, ids, ids_looked, dense, tables, w1, b1, w2, b2, w3, y):
    batch = dense.shape[0]
    TILES = batch // P
    H1, H2 = w1.shape[2], w2.shape[1]
    M1, M2 = H1 // P, H2 // P
    ROWS = tables[LOOKED[0]].shape[0] // ROW_TILES
    assert all(tables[f].shape[0] == ROWS * ROW_TILES and ROWS <= P for f in LOOKED)

    with ExitStack() as ctx:
        def sb(name, shape, dt=F32):
            return ctx.enter_context(nc.sbuf_tensor(name, shape, dt))

        def ps(name, shape):
            return ctx.enter_context(nc.psum_tensor(name, shape, F32))

        def sem(name):
            return ctx.enter_context(nc.semaphore(name))

        ids_sb = [sb(f"ids_sb{k}", [P, N_FEAT], U32) for k in range(2)]
        X = sb("X", [P, N_FEAT, DEPTH])
        XT = [sb(f"XT{k}", [P, HALVES, P, N_FEAT]) for k in range(2)]
        table_hi = [sb(f"table_hi{n}", [P, ROW_TILES, DEPTH], F32R) for n in range(N_LOOK)]
        table_lo = [sb(f"table_lo{n}", [P, ROW_TILES, DEPTH], F32R) for n in range(N_LOOK)]
        stage = XT[1][:, :, :, :].rearrange("p h b f -> p (h b f)")[:, 0:N_LOOK * ROW_TILES * DEPTH].rearrange(
            "p (n r d) -> p n r d", n=N_LOOK, r=ROW_TILES)
        row_of = sb("row_of", [P, ROW_TILES])
        ids_all = [sb(f"ids_all{k}", [P, N_LOOK, P], mybir.dt.int32) for k in range(2)]
        onehot = [sb(f"onehot{k}", [P, ROW_TILES, P], F32R) for k in range(2)]
        Z = sb("Z", [P, N_FEAT, QUADS])
        T = sb("T", [P, N_FEAT, N_FEAT])
        C = sb("C", [P, K_TILES * P])
        TT = sb("TT", [P, K_TILES, P])
        h1 = sb("h1", [P, M1, P])
        h2 = sb("h2", [P, M2, P])
        y_sb = sb("y_sb", [1, batch])
        dense_sb = sb("dense_sb", [P, TILES, N_DENSE])
        w1_sb = sb("w1_sb", [P, K_TILES, H1])
        w2_sb = sb("w2_sb", [P, M1, H2])
        w3_sb = sb("w3_sb", [P, M2])
        b1_sb = sb("b1_sb", [P, M1])
        b2_sb = sb("b2_sb", [P, M2])
        ident = sb("ident", [P, P])

        xt_ps = [ps(f"xt_ps{k}", [P, 2, HALVES, P]) for k in range(2)]
        dots_ps = [ps(f"dots_ps{k}", [P, GROUP, P]) for k in range(2)]
        look_ps = [ps(f"look_ps{k}", [P, 2, DEPTH]) for k in range(2)]
        bank_a = ps("bank_a", [P, 4, P])
        bank_b = ps("bank_b", [P, 4, P])
        banks = [bank_a, bank_b]

        tables_landed = [sem(f"tables_landed{n}") for n in range(N_LOOK)]
        hi_ready = sem("hi_ready")
        lo_ready = sem("lo_ready")
        row_of_ready = sem("row_of_ready")
        ids_all_landed = [sem(f"ids_all_landed{k}") for k in range(2)]
        onehot_ready = sem("onehot_ready")
        looked_up = sem("looked_up")
        x_by_act = sem("x_by_act")
        ids_landed = [sem(f"ids_landed{k}") for k in range(2)]
        gathered = [sem(f"gathered{f}") for f in range(N_FEAT)]
        dense_landed = sem("dense_landed")
        w1_landed = sem("w1_landed")
        w2_landed = sem("w2_landed")
        small_landed = sem("small_landed")
        ident_zeroed = sem("ident_zeroed")
        ident_ready = sem("ident_ready")
        ids_waited = sem("ids_waited")
        slots_waited = sem("slots_waited")
        turned = sem("turned")
        xt_by_dve = sem("xt_by_dve")
        xt_by_act = sem("xt_by_act")
        dots_done = sem("dots_done")
        z_by_dve = sem("z_by_dve")
        z_by_act = sem("z_by_act")
        z_turned = sem("z_turned")
        c_by_act = sem("c_by_act")
        c_turned = sem("c_turned")
        banks_free = sem("banks_free")
        tt_by_dve = sem("tt_by_dve")
        tt_by_act = sem("tt_by_act")
        h1_summed = sem("h1_summed")
        h1_ready = sem("h1_ready")
        h2_summed = sem("h2_summed")
        h2_ready = sem("h2_ready")
        y_summed = sem("y_summed")
        y_stored = sem("y_stored")

        y_q = y_sb[:, :].rearrange("o (t q j) -> o t j q", q=QUADS, j=4)
        ids_rows = ids_looked.rearrange("(o n) (t b) -> t o n b", o=1, b=P).broadcast_to([TILES, P, N_LOOK, P])
        ids_tiles = ids.bitcast(U32).rearrange("(t p) f -> t p f", p=P)

        block = ctx.enter_context(nc.Block())

        @block.sync
        def _(sp):
            def load_ids(t, k):
                sp.dma_start(ids_sb[k][:, :], ids_tiles[t]).then_inc(ids_landed[k], 16)
                sp.dma_start(ids_all[k][:, :, :], ids_rows[t]).then_inc(ids_all_landed[k], 16)

            for t in range(2):
                load_ids(t, t)
            for n, f in enumerate(LOOKED):
                sp.dma_start(stage[0:ROWS, n], tables[f].rearrange("(r p) d -> p r d", p=ROWS)
                             ).then_inc(tables_landed[n], 16)
            dense_q = dense.rearrange("(t q j) c -> j q t c", j=4, q=QUADS)
            for j in range(4):
                sp.dma_start(dense_sb[32 * j:32 * j + 32, :, :], dense_q[j]).then_inc(dense_landed, 16)
            sp.dma_start(w1_sb[:, :, :], w1.rearrange("k p n -> p k n")).then_inc(w1_landed, 16)
            sp.dma_start(w2_sb[:, :, :], w2.rearrange("(k p) n -> p k n", p=P)).then_inc(w2_landed, 16)
            sp.dma_start(b1_sb[:, :], b1).then_inc(small_landed, 16)
            sp.dma_start(b2_sb[:, :], b2).then_inc(small_landed, 16)
            sp.dma_start(w3_sb[:, :], w3).then_inc(small_landed, 16)
            with sp.Fori(1, TILES // 2) as i:
                for k in range(2):
                    sp.wait_ge(turned, PAIRS * (2 * i + k - 1))
                    load_ids(2 * i + k, k)
            sp.wait_ge(banks_free, TILES + 1)
            sp.dma_start(y.rearrange("b o -> o b"), y_sb[:, :]).then_inc(y_stored, 16)
            sp.wait_ge(y_stored, 16)

        @block.gpsimd
        def _(pool):
            def gather_tile(t, k, first=False):
                pool.wait_ge(ids_landed[k], 8 * (t - k) + 16)
                pool.sem_inc(ids_waited, 1)
                for f in range(N_FEAT):
                    if not first and f % SLOTS == 0:
                        pool.wait_ge(turned, PAIRS * (t - 1) + (f + SLOTS) // 2)
                        pool.sem_inc(slots_waited, 1)
                    if f in LOOKED:
                        continue
                    pool.indirect_dma_start(
                        X[:, f, :], None, tables[f], bass.IndirectOffsetOnAxis(ids_sb[k][:, f:f + 1], 0)
                    ).then_inc(gathered[f], 16)

            pool.memset(ident[:, :], 0.0).then_inc(ident_zeroed, 1)
            pool.wait_ge(ident_zeroed, 1)
            pool.affine_select(out=ident[:, :], in_=ident[:, :], compare_op=ALU.not_equal, fill=1.0,
                               base=0, pattern=[[-1, P]], channel_multiplier=1).then_inc(ident_ready, 1)
            pool.iota(row_of[:, :], pattern=[[ROWS, ROW_TILES]], base=0, channel_multiplier=1,
                      allow_small_or_imprecise_dtypes=True).then_inc(row_of_ready, 1)
            gather_tile(0, 0, first=True)
            with pool.Fori(1, TILES // 2) as i:
                gather_tile(2 * i - 1, 1)
                gather_tile(2 * i, 0)
            gather_tile(TILES - 1, 1)

        @block.tensor
        def _(pe):
            def turn_pair(t, pair, first=False):
                if not (first and pair < 2):
                    pe.wait_ge((xt_by_dve, xt_by_act)[pair % 2], PAIRS // 2 * t + pair // 2)
                for e in range(2):
                    f = 2 * pair + e
                    if f in LOOKED:
                        pe.wait_ge(x_by_act, N_LOOK * t + LOOKED.index(f) + 1)
                    else:
                        pe.wait_ge(gathered[f], 16 * (t + 1))
                    for h in range(HALVES):
                        last = pe.transpose(xt_ps[pair % 2][:, e, h, :], X[:, f, h * P:(h + 1) * P], ident[:, :])
                last.then_inc(turned, 1)

            def look_up(t, k, n):
                at = N_LOOK * t + n
                b = (k + n) % 2
                pe.wait_ge(onehot_ready, at + 1)
                if not (k == 0 and n < 2 and type(t) is int and t == 0):
                    pe.wait_ge(x_by_act, at - 1)
                parts = [(part, r) for part in (table_hi[n], table_lo[n]) for r in range(ROW_TILES)]
                for part, r in parts:
                    last = pe.matmul(look_ps[b][:, 0, :], onehot[b][0:ROWS, r, :], part[0:ROWS, r, :],
                                     start=(part, r) == parts[0], stop=(part, r) == parts[-1])
                last.then_inc(looked_up, 1)

            def dots_group(u, k, g, first=False):
                if g == 0:
                    pe.wait_ge(xt_by_dve, PAIRS // 2 * (u + 1))
                    pe.wait_ge(xt_by_act, PAIRS // 2 * (u + 1))
                if not (first and g < 2):
                    pe.wait_ge(z_by_dve, GROUPS * u + g - 1)
                    pe.wait_ge(z_by_act, GROUPS * u + g - 1)
                for quad in range(GROUP):
                    for h in range(HALVES):
                        for c in range(2):
                            b = 4 * (GROUP * g + quad) + 2 * c
                            rows = XT[k][:, h, b:b + 2, :].rearrange("p j f -> p (j f)")
                            lanes = slice(64 * c, 64 * c + 64)
                            last = pe.matmul(dots_ps[g % 2][lanes, quad, lanes], rows, rows,
                                             start=(h == 0), stop=(h == HALVES - 1))
                last.then_inc(dots_done, 1)

            def turn_c(u):
                pe.wait_ge(c_by_act, u + 2)
                pe.wait_ge(banks_free, u + 1)
                for n in range(K_TILES):
                    out = bank_a[:, n, :] if n < 4 else bank_b[:, 0, :]
                    last = pe.transpose(out, C[:, n * P:(n + 1) * P], ident[:, :])
                last.then_inc(c_turned, 1)

            def layer1(u, chunks):
                for m in chunks:
                    if m == 0:
                        pe.wait_ge(tt_by_dve, u + 1)
                        pe.wait_ge(tt_by_act, u + 1)
                    if m >= 2:
                        pe.wait_ge(h1_ready, M1 * u + m - 1)
                    for k in range(K_TILES):
                        last = pe.matmul(banks[m % 2][:, m, :], w1_sb[:, k, m * P:(m + 1) * P], TT[:, k, :],
                                         start=(k == 0), stop=(k == K_TILES - 1))
                    last.then_inc(h1_summed, 1)

            def layer2(u):
                pe.wait_ge(h1_ready, M1 * (u + 1))
                for m in range(M2):
                    for k in range(M1):
                        last = pe.matmul(banks[m % 2][:, m, :], w2_sb[:, k, m * P:(m + 1) * P], h1[:, k, :],
                                         start=(k == 0), stop=(k == M1 - 1))
                    last.then_inc(h2_summed, 1)

            def layer3(u):
                pe.wait_ge(h2_ready, M2 * (u + 1))
                for k in range(M2):
                    last = pe.matmul(bank_a[0:1, 3, :], w3_sb[:, k:k + 1], h2[:, k, :],
                                     start=(k == 0), stop=(k == M2 - 1))
                last.then_inc(y_summed, 1)

            def layers_after(pair, u):
                if pair == 4:
                    turn_c(u)
                if pair in (6, 7, 8, 9):
                    layer1(u, [pair - 6])
                if pair == 12:
                    layer2(u)
                if pair == 14:
                    layer3(u)

            def tile_step(t, k, dots=True, layered=True, look=True):
                for pair in range(PAIRS):
                    turn_pair(t, pair, not dots)
                    if dots and pair % 2 == 1:
                        dots_group(t - 1, 1 - k, pair // 2, not layered)
                    if layered:
                        layers_after(pair, t - 2)
                    if look and pair in (3, 7, 11):
                        look_up(t + 1, 1 - k, pair // 4)

            pe.sem_inc(c_turned, 1)
            pe.wait_ge(ident_ready, 1)
            pe.wait_ge(lo_ready, N_LOOK)
            pe.wait_ge(hi_ready, N_LOOK)
            for n in range(N_LOOK):
                look_up(0, 0, n)
            tile_step(0, 0, dots=False, layered=False)
            tile_step(1, 1, layered=False)
            pe.wait_ge(w1_landed, 16)
            pe.wait_ge(w2_landed, 16)
            pe.wait_ge(small_landed, 48)
            with pe.Fori(1, TILES // 2 - 1) as i:
                tile_step(2 * i, 0)
                tile_step(2 * i + 1, 1)
            tile_step(TILES - 2, 0)
            tile_step(TILES - 1, 1, look=False)
            for pair in range(PAIRS):
                if pair % 2 == 1:
                    dots_group(TILES - 1, 1, pair // 2)
                layers_after(pair, TILES - 2)
            turn_c(TILES - 1)
            layer1(TILES - 1, range(M1))
            layer2(TILES - 1)
            layer3(TILES - 1)

        def copy_dots(engine_copy, g, j):
            lanes = slice(32 * j, 32 * j + 32)
            src = dots_ps[g % 2][lanes, :, 32 * j:32 * j + 32]
            dst = Z[lanes, :, g * GROUP:(g + 1) * GROUP].rearrange("p m q -> p q m")
            return engine_copy(dst, src)

        def copy_turned(engine_copy, k, pair):
            dst = XT[k][:, :, :, 2 * pair:2 * pair + 2].rearrange("p h b e -> p e h b")
            return engine_copy(dst, xt_ps[pair % 2][:, :, :, :])

        @block.vector
        def _(dve):
            def copy(dst, src):
                return dve.tensor_copy(dst, src)

            def even_pair(t, k, pair, early=False):
                dve.wait_ge(turned, PAIRS * t + pair + 1)
                if pair == 0 and not early:
                    dve.wait_ge(dots_done, GROUPS * (t - 1))
                copy_turned(copy, k, pair).then_inc(xt_by_dve, 1)

            def dots_group(u, g, first=False):
                dve.wait_ge(dots_done, GROUPS * u + g + 1)
                if g == 0 and not first:
                    dve.wait_ge(z_turned, u)
                copy_dots(copy, g, 0)
                copy_dots(copy, g, 1).then_inc(z_by_dve, 1)

            def turn_z(u):
                dve.wait_ge(z_by_dve, GROUPS * (u + 1))
                dve.wait_ge(z_by_act, GROUPS * (u + 1))
                dve.wait_ge(c_by_act, u + 1)
                dve.transpose(T[:, :, :], Z[:, :, :]).then_inc(z_turned, 1)

            def operand(u):
                dve.wait_ge(c_turned, u + 2)
                dve.tensor_copy(TT[:, 0:4, :], bank_a[:, :, :]).then_inc(tt_by_dve, 1)

            def make_onehot(t, k, n):
                at = N_LOOK * t + n
                if n == 0:
                    dve.wait_ge(ids_all_landed[k], 8 * (t - k) + 16)
                if not (k == 0 and n < 2 and type(t) is int and t == 0):
                    dve.wait_ge(looked_up, at - 1)
                dve.tensor_tensor(onehot[(k + n) % 2][:, :, :],
                                  ids_all[k][:, n:n + 1, :].broadcast_to([P, ROW_TILES, P]),
                                  row_of[:, :].rearrange("p (r o) -> p r o", o=1).broadcast_to([P, ROW_TILES, P]),
                                  ALU.is_equal).then_inc(onehot_ready, 1)

            def tile_step(t, k, dots=True, layered=True, look=True):
                for pair in range(0, PAIRS, 2):
                    even_pair(t, k, pair, not layered)
                    if look and pair in (0, 4, 8):
                        make_onehot(t + 1, 1 - k, pair // 4)
                    if layered and pair == 0:
                        turn_z(t - 2)
                    if layered and pair == 4:
                        operand(t - 2)
                    if dots:
                        dots_group(t - 1, pair // 2, not layered)

            for n in range(N_LOOK):
                dve.wait_ge(hi_ready, n + 1)
                dve.tensor_tensor(table_lo[n][0:ROWS], stage[0:ROWS, n], table_hi[n][0:ROWS].bitcast(F32),
                                  ALU.subtract).then_inc(lo_ready, 1)
            dve.wait_ge(row_of_ready, 1)
            for n in range(N_LOOK):
                make_onehot(0, 0, n)
            tile_step(0, 0, dots=False, layered=False)
            dve.wait_ge(lo_ready, N_LOOK)
            tile_step(1, 1, layered=False)
            with dve.Fori(1, TILES // 2 - 1) as i:
                tile_step(2 * i, 0)
                tile_step(2 * i + 1, 1)
            tile_step(TILES - 2, 0)
            tile_step(TILES - 1, 1, look=False)
            turn_z(TILES - 2)
            for g in range(GROUPS):
                dots_group(TILES - 1, g)
                if g == 2:
                    operand(TILES - 2)
            turn_z(TILES - 1)
            operand(TILES - 1)

        @block.scalar
        def _(act):
            def copy(dst, src):
                return act.activation(dst, src, ACT.Copy)

            def odd_pair(t, k, pair, early=False):
                act.wait_ge(turned, PAIRS * t + pair + 1)
                if pair == 1 and not early:
                    act.wait_ge(dots_done, GROUPS * (t - 1))
                copy_turned(copy, k, pair).then_inc(xt_by_act, 1)

            def dots_group(u, g, first=False):
                act.wait_ge(dots_done, GROUPS * u + g + 1)
                if g == 0 and not first:
                    act.wait_ge(z_turned, u)
                copy_dots(copy, g, 2)
                copy_dots(copy, g, 3).then_inc(z_by_act, 1)

            def pick(u):
                corners = C[:, CORNERS:].rearrange("p (a m i) -> p a m i", a=2, i=8)
                act.wait_ge(c_turned, u + 1)
                copy(corners[:, :, 0, :], dense_sb[:, u, :].rearrange("p (a c) -> p a c", a=2))
                act.wait_ge(z_turned, u + 1)
                copy(C[:, 0:LATE].rearrange("p (m i) -> p m i", i=16), T[:, 8:32, 0:16])
                copy(C[:, LATE:CORNERS].rearrange("p (m i) -> p m i", i=16), T[:, 24:32, 16:32])
                copy(corners[:, 0, 1:8, :], T[:, 1:8, 0:8])
                copy(corners[:, 1, 1:8, :], T[:, 17:24, 16:24]).then_inc(c_by_act, 1)

            def operand(u):
                act.wait_ge(c_turned, u + 2)
                copy(TT[:, 4, :], bank_b[:, 0, :]).then_inc(tt_by_act, 1)

            def relu1(u, chunks):
                for m in chunks:
                    act.wait_ge(h1_summed, M1 * u + m + 1)
                    act.activation(h1[:, m, :], banks[m % 2][:, m, :], ACT.Relu, bias=b1_sb[:, m:m + 1]).then_inc(h1_ready, 1)

            def relu2(u):
                for m in range(M2):
                    act.wait_ge(h2_summed, M2 * u + m + 1)
                    act.activation(h2[:, m, :], banks[m % 2][:, m, :], ACT.Relu, bias=b2_sb[:, m:m + 1]).then_inc(h2_ready, 1)

            def out(u):
                act.wait_ge(y_summed, u + 1)
                copy(y_q[:, u, :, :], bank_a[0:1, 3, :].rearrange("o (j q) -> o j q", j=4)).then_inc(banks_free, 1)

            def layers_after(pair, u):
                if pair == 1:
                    pick(u)
                if pair == 5:
                    operand(u)
                if pair == 7:
                    relu1(u, [0])
                if pair == 9:
                    relu1(u, [1, 2])
                if pair == 11:
                    relu1(u, [3])
                if pair == 13:
                    relu2(u)
                if pair == 15:
                    out(u)

            def store_looked(t, k, n):
                act.wait_ge(looked_up, N_LOOK * t + n + 1)
                copy(X[:, LOOKED[n], :], look_ps[(k + n) % 2][:, 0, :]).then_inc(x_by_act, 1)

            def tile_step(t, k, dots=True, layered=True, look=True):
                for pair in range(1, PAIRS, 2):
                    odd_pair(t, k, pair, not layered)
                    if layered:
                        layers_after(pair, t - 2)
                    if look and pair in (5, 9, 13):
                        store_looked(t + 1, 1 - k, pair // 4 - 1)
                    if dots:
                        dots_group(t - 1, pair // 2, not layered)

            act.sem_inc(banks_free, 1)
            act.sem_inc(c_by_act, 1)
            for n in range(N_LOOK):
                act.wait_ge(tables_landed[n], 16)
                copy(table_hi[n][0:ROWS], stage[0:ROWS, n]).then_inc(hi_ready, 1)
            for n in range(N_LOOK):
                store_looked(0, 0, n)
            tile_step(0, 0, dots=False, layered=False)
            act.wait_ge(lo_ready, N_LOOK)
            tile_step(1, 1, layered=False)
            act.wait_ge(dense_landed, 64)
            act.wait_ge(small_landed, 48)
            with act.Fori(1, TILES // 2 - 1) as i:
                tile_step(2 * i, 0)
                tile_step(2 * i + 1, 1)
            tile_step(TILES - 2, 0)
            tile_step(TILES - 1, 1, look=False)
            for pair in range(1, PAIRS, 2):
                layers_after(pair, TILES - 2)
                dots_group(TILES - 1, pair // 2)
            pick(TILES - 1)
            operand(TILES - 1)
            relu1(TILES - 1, range(M1))
            relu2(TILES - 1)
            out(TILES - 1)


def kernel(**inputs):
    import numpy as np
    import concourse.bacc as bacc
    from concourse.bass_utils import run_bass_kernel_spmd

    nc = bacc.Bacc("TRN2", target_bir_lowering=False, num_devices=1)
    arrays = {}

    def given(name, a):
        a = np.ascontiguousarray(a)
        arrays[name] = a
        return nc.dram_tensor(name, a.shape, mybir.dt.from_np(a.dtype), kind="ExternalInput").ap()

    w_top1 = np.asarray(inputs["W_top1"])
    w1 = np.zeros((K_TILES * P, w_top1.shape[1]), w_top1.dtype)
    rows = np.array(pair_rows())
    w1[rows >= 0] = w_top1[rows[rows >= 0]]

    ids = given("ids", inputs["ids"])
    ids_looked = given("ids_looked", np.asarray(inputs["ids"])[:, list(LOOKED)].T)
    dense = given("dense_ctx", inputs["dense_ctx"])
    tables = [given(f"tbl_{f}", inputs[f"tbl_{f}"]) for f in range(N_FEAT)]
    w1 = given("w1", w1.reshape(K_TILES, P, -1))
    b1 = given("b1", np.asarray(inputs["b_top1"]).reshape(-1, P).T)
    w2 = given("w2", inputs["W_top2"])
    b2 = given("b2", np.asarray(inputs["b_top2"]).reshape(-1, P).T)
    w3 = given("w3", np.asarray(inputs["W_top3"]).reshape(-1, P).T)
    y = nc.dram_tensor("y", (dense.shape[0], 1), F32, kind="ExternalOutput").ap()
    build(nc, ids, ids_looked, dense, tables, w1, b1, w2, b2, w3, y)
    result = run_bass_kernel_spmd(nc, [arrays], core_ids=[0])
    return result.results[0]["y"]
```

```python
from contextlib import ExitStack

import concourse.bass as bass
from concourse import mybir

P = 128
F32 = mybir.dt.float32
F32R = mybir.dt.float32r
U32 = mybir.dt.uint32
ALU = mybir.AluOpType
ACT = mybir.ActivationFunctionType

N_FEAT = 32
DEPTH = 256
HALVES = DEPTH // P
N_DENSE = 16
QUADS = P // 4
GROUP = 4
GROUPS = QUADS // GROUP
LOOKED = (1, 6, 18, 23)
N_LOOK = len(LOOKED)
CHUNKS = 2 * N_LOOK
GATHERED = tuple(f for f in range(N_FEAT) if f not in LOOKED)
N_GATHER = len(GATHERED)
PAIRS = N_GATHER // 2
ROW_TILES = 8
HALF_ROWS = ROW_TILES // 2
DOTS_AFTER = ({1: 0, 4: 2, 7: 4, 10: 6}, {1: 0, 3: 2, 5: 4, 7: 6})
LAYER1_AFTER = {5: 0, 6: 1, 8: 2, 9: 3}
LAYER2_AFTER = (11, 10)
LAYER3_AFTER = (13, 12)
LOOK_AFTER = ({5: 6, 8: 7}, {8: 0, 9: 1, 10: 2, 11: 3, 12: 4, 13: 5})
LOOK_AFTER_0 = {0: 2, 1: 3, 3: 4, 4: 5, 6: 6, 7: 7}
DOTS_AFTER_1 = {0: 0, 1: 2, 2: 4, 3: 6}
LOOK_AFTER_1 = {4: 0, 5: 1, 7: 2, 8: 3, 10: 4, 11: 5}


def chunk_after(k, pair, dots, layered):
    return (LOOK_AFTER[k] if layered else LOOK_AFTER_1 if dots else LOOK_AFTER_0).get(pair)


def dots_after(k, pair, dots, layered):
    g = ((DOTS_AFTER[k] if layered else DOTS_AFTER_1) if dots else {}).get(pair)
    return () if g is None else (g, g + 1)


K_TILES = 4
B = 8


PARTS = ((8, 16, 0, 8), (16, 32, 0, 16), (24, 32, 16, 24), (8, 16, 8, 16), (24, 32, 24, 32))
N_SQUARES = 2


def operand_rows():
    def row(i, m):
        return i * (2 * N_FEAT - i - 1) // 2 + (m - i - 1)

    n_pairs = N_FEAT * (N_FEAT - 1) // 2
    rows = []
    for n, (m0, m1, i0, i1) in enumerate(PARTS):
        square = n - (len(PARTS) - N_SQUARES)
        for m in range(m0, m1):
            for i in range(i0, i1):
                if square < 0:
                    rows.append(row(i, m))
                elif m == i:
                    rows.append(n_pairs + B * square + m - m0)
                elif m < i:
                    rows.append(row(m, i))
                else:
                    rows.append(row(i - B, m - B))
    assert sorted(rows) == list(range(n_pairs + N_DENSE))
    return rows


def build(nc, ids, ids_looked, dense, tables, w1, b1, w2, b2, w3, y):
    batch = dense.shape[0]
    TILES = batch // P
    H1, H2 = w1.shape[2], w2.shape[1]
    M1, M2 = H1 // P, H2 // P
    ROWS = tables[LOOKED[0]].shape[0] // ROW_TILES
    assert all(tables[f].shape[0] == ROWS * ROW_TILES and ROWS <= P for f in LOOKED)

    with ExitStack() as ctx:
        def sb(name, shape, dt=F32):
            return ctx.enter_context(nc.sbuf_tensor(name, shape, dt))

        def ps(name, shape):
            return ctx.enter_context(nc.psum_tensor(name, shape, F32))

        def sem(name):
            return ctx.enter_context(nc.semaphore(name))

        ids_sb = [sb(f"ids_sb{k}", [P, N_FEAT], U32) for k in range(2)]
        X = sb("X", [P, N_GATHER, DEPTH])
        XT = [sb(f"XT{k}", [P, HALVES, P, N_FEAT]) for k in range(2)]
        looked_next = sb("looked_next", [P, N_LOOK, HALVES, P])
        table_hi = [sb(f"table_hi{n}", [P, ROW_TILES, DEPTH], F32R) for n in range(N_LOOK)]
        table_lo = [sb(f"table_lo{n}", [P, ROW_TILES, DEPTH], F32R) for n in range(N_LOOK)]
        wide = XT[1][:, :, :, :].rearrange("p h b f -> p (h b f)").rearrange("p (n r d) -> p n r d", r=ROW_TILES, d=DEPTH)
        stage = [wide[:, n] for n in range(N_LOOK)]
        row_of = sb("row_of", [P, ROW_TILES])
        ids_all = sb("ids_all", [P, N_LOOK, 2 * P], mybir.dt.int32)
        onehot = [sb(f"onehot{c}", [P, HALF_ROWS, 2 * P], F32R) for c in range(2)]
        Z = sb("Z", [P, N_FEAT, QUADS])
        T = sb("T", [P, N_FEAT, N_FEAT])
        C = sb("C", [P, K_TILES * P])
        TT = sb("TT", [P, K_TILES, P])
        h1 = sb("h1", [P, M1, P])
        h2 = sb("h2", [P, M2, P])
        y_sb = sb("y_sb", [1, P])
        dense_sb = sb("dense_sb", [P, TILES, N_DENSE])
        w1_sb = sb("w1_sb", [P, K_TILES, H1])
        w2_sb = sb("w2_sb", [P, M1, H2])
        w3_sb = sb("w3_sb", [P, M2])
        b1_sb = sb("b1_sb", [P, M1])
        b2_sb = sb("b2_sb", [P, M2])
        ident = sb("ident", [P, P])
        below = sb("below", [P, N_SQUARES, B, B])

        xt_ps = [ps(f"xt_ps{k}", [P, 2, HALVES, P]) for k in range(2)]
        dots_ps = [ps(f"dots_ps{k}", [P, GROUP, P]) for k in range(2)]
        look_ps = [ps(f"look_ps{h}", [P, 2, 2 * P]) for h in range(HALVES)]
        last_banks = [b[:, :, :].rearrange("p a (c n) -> p (a c) n", n=P) for b in look_ps]
        bank_a = ps("bank_a", [P, 4, P])
        bank_b = ps("bank_b", [P, 4, P])
        banks = [bank_a[:, :, :], bank_b[:, :, :]]

        tables_landed = [sem(f"tables_landed{n}") for n in range(N_LOOK)]
        hi_ready = sem("hi_ready")
        lo_ready = sem("lo_ready")
        row_of_ready = sem("row_of_ready")
        ids_all_landed = sem("ids_all_landed")
        onehot_ready = sem("onehot_ready")
        looked_up = sem("looked_up")
        looked_by_act = sem("looked_by_act")
        looked_moved = sem("looked_moved")
        ids_landed = [sem(f"ids_landed{k}") for k in range(2)]
        gathered = [sem(f"gathered{n}") for n in range(N_GATHER)]
        dense_landed = sem("dense_landed")
        w1_landed = sem("w1_landed")
        w2_landed = sem("w2_landed")
        small_landed = sem("small_landed")
        ident_zeroed = sem("ident_zeroed")
        ident_ready = sem("ident_ready")
        t_waited = sem("t_waited")
        ids_waited = sem("ids_waited")
        slots_waited = sem("slots_waited")
        turned = sem("turned")
        xt_by_dve = sem("xt_by_dve")
        xt_by_act = sem("xt_by_act")
        dots_done = sem("dots_done")
        z_by_dve = sem("z_by_dve")
        z_by_act = sem("z_by_act")
        z_turned = sem("z_turned")
        squares_set = sem("squares_set")
        t_ready = sem("t_ready")
        below_ready = sem("below_ready")
        c_by_act = sem("c_by_act")
        c_by_dve = sem("c_by_dve")
        c_turned = sem("c_turned")
        banks_free = sem("banks_free")
        tt_by_dve = sem("tt_by_dve")
        tt_by_act = sem("tt_by_act")
        h1_summed = sem("h1_summed")
        h1_ready = sem("h1_ready")
        h2_summed = sem("h2_summed")
        h2_ready = sem("h2_ready")
        y_summed = sem("y_summed")
        y_stored = sem("y_stored")

        y_q = y_sb[:, :].rearrange("o (q j) -> o j q", q=QUADS, j=4)
        y_tiles = y.rearrange("(t b) o -> t o b", b=P)
        ids_rows = ids_looked.rearrange("(o n) (i b) -> i o n b", o=1, b=2 * P).broadcast_to([TILES // 2, P, N_LOOK, 2 * P])
        ids_tiles = ids.bitcast(U32).rearrange("(t p) f -> t p f", p=P)

        block = ctx.enter_context(nc.Block())

        @block.sync
        def _(sp):
            def load_ids(t, k):
                sp.dma_start(ids_sb[k][:, :], ids_tiles[t]).then_inc(ids_landed[k], 16)

            def load_ids_all(i):
                sp.dma_start(ids_all[:, :, :], ids_rows[i]).then_inc(ids_all_landed, 16)

            sp.sem_inc(y_stored, 16)
            load_ids(0, 0)
            load_ids_all(0)
            load_ids(1, 1)
            for n, f in enumerate(LOOKED):
                sp.dma_start(stage[n][0:ROWS], tables[f].rearrange("(r p) d -> p r d", p=ROWS)
                             ).then_inc(tables_landed[n], 16)
            dense_q = dense.rearrange("(t q j) c -> j q t c", j=4, q=QUADS)
            for j in range(4):
                sp.dma_start(dense_sb[32 * j:32 * j + 32, :, :], dense_q[j]).then_inc(dense_landed, 16)
            sp.dma_start(w1_sb[:, :, :], w1.rearrange("k p n -> p k n")).then_inc(w1_landed, 16)
            sp.dma_start(w2_sb[:, :, :], w2.rearrange("(k p) n -> p k n", p=P)).then_inc(w2_landed, 16)
            sp.dma_start(b1_sb[:, :], b1).then_inc(small_landed, 16)
            sp.dma_start(b2_sb[:, :], b2).then_inc(small_landed, 16)
            sp.dma_start(w3_sb[:, :], w3).then_inc(small_landed, 16)

            def next_ids(t, k):
                sp.wait_ge(turned, PAIRS * (t - 1))
                load_ids(t, k)

            def store_y(u):
                sp.wait_ge(banks_free, u + 2)
                sp.dma_start(y_tiles[u], y_sb[:, :]).then_inc(y_stored, 16)

            next_ids(2, 0)
            load_ids_all(1)
            next_ids(3, 1)
            with sp.Fori(2, TILES // 2) as i:
                for k in range(2):
                    next_ids(2 * i + k, k)
                    if k == 0:
                        load_ids_all(i)
                    store_y(2 * i + k - 4)
            for u in range(TILES - 4, TILES):
                store_y(u)
            sp.wait_ge(y_stored, 16 * (TILES + 1))

        @block.gpsimd
        def _(pool):
            def gather_tile(t, k, first=False):
                pool.wait_ge(ids_landed[k], 8 * (t - k) + 16)
                pool.sem_inc(ids_waited, 1)
                for g, f in enumerate(GATHERED):
                    if g % 2 == 0 and not first:
                        pool.wait_ge(turned, PAIRS * (t - 1) + g // 2 + 1)
                        pool.sem_inc(slots_waited, 1)
                    pool.indirect_dma_start(
                        X[:, g, :], None, tables[f], bass.IndirectOffsetOnAxis(ids_sb[k][:, f:f + 1], 0)
                    ).then_inc(gathered[g], 16)

            pool.memset(ident[:, :], 0.0).then_inc(ident_zeroed, 1)
            pool.wait_ge(ident_zeroed, 1)
            pool.affine_select(out=ident[:, :], in_=ident[:, :], compare_op=ALU.not_equal, fill=1.0,
                               base=0, pattern=[[-1, P]], channel_multiplier=1).then_inc(ident_ready, 1)
            pool.memset(below[:, :, :, :], 1.0).then_inc(below_ready, 1)
            pool.wait_ge(below_ready, 1)
            pool.affine_select(out=below[:, :, :, :], in_=below[:, :, :, :], compare_op=ALU.is_gt, fill=0.0, base=0,
                               pattern=[[0, N_SQUARES], [1, B], [-1, B]], channel_multiplier=0).then_inc(below_ready, 1)
            pool.iota(row_of[:, :], pattern=[[ROWS, ROW_TILES]], base=0, channel_multiplier=1,
                      allow_small_or_imprecise_dtypes=True).then_inc(row_of_ready, 1)
            gather_tile(0, 0, first=True)
            with pool.Fori(1, TILES // 2) as i:
                gather_tile(2 * i - 1, 1)
                gather_tile(2 * i, 0)
            gather_tile(TILES - 1, 1)

        @block.tensor
        def _(pe):
            def turn_pair(t, pair, first=False):
                if not (first and pair < 2):
                    pe.wait_ge((xt_by_dve, xt_by_act)[pair % 2], PAIRS // 2 * t + pair // 2)
                for e in range(2):
                    g = 2 * pair + e
                    pe.wait_ge(gathered[g], 16 * (t + 1))
                    for h in range(HALVES):
                        last = pe.transpose(xt_ps[pair % 2][:, e, h, :], X[:, g, h * P:(h + 1) * P], ident[:, :])
                last.then_inc(turned, 1)

            def look_up(t, q, first=False):
                n, c = q // 2, q % 2
                pe.wait_ge(onehot_ready, N_LOOK * t + q + 1)
                if first:
                    pe.wait_ge(hi_ready, n + 1)
                    pe.wait_ge(lo_ready, n + 1)
                if c == 0 and not (first and n == 0):
                    pe.wait_ge(looked_by_act, N_LOOK // 2 * t + n)
                parts = [(part, r) for part in (table_hi[n], table_lo[n]) for r in range(HALF_ROWS)]
                for h in range(HALVES):
                    for part, r in parts:
                        rows = part[0:ROWS, HALF_ROWS * c + r, h * P:(h + 1) * P]
                        last = pe.matmul(look_ps[h][:, 0, :], rows, onehot[c][0:ROWS, r, :],
                                         start=c == 0 and (part, r) == parts[0],
                                         stop=c == 1 and (part, r) == parts[-1])
                last.then_inc(looked_up, 1)

            def dots_group(u, k, g, first=False):
                if g == 0:
                    pe.wait_ge(xt_by_dve, PAIRS // 2 * (u + 1))
                    pe.wait_ge(xt_by_act, PAIRS // 2 * (u + 1))
                    if k == 0:
                        pe.wait_ge(looked_by_act, N_LOOK // 2 * u + N_LOOK)
                    else:
                        pe.wait_ge(looked_moved, u + 1)
                if not (first and g < 2):
                    pe.wait_ge(z_by_dve, GROUPS * u + g - 1)
                    pe.wait_ge(z_by_act, GROUPS * u + g - 1)
                for quad in range(GROUP):
                    for h in range(HALVES):
                        for c in range(2):
                            b = 4 * (GROUP * g + quad) + 2 * c
                            rows = XT[k][:, h, b:b + 2, :].rearrange("p j f -> p (j f)")
                            lanes = slice(64 * c, 64 * c + 64)
                            last = pe.matmul(dots_ps[g % 2][lanes, quad, lanes], rows, rows,
                                             start=(h == 0), stop=(h == HALVES - 1))
                last.then_inc(dots_done, 1)

            def turn_c(u, banks=banks):
                pe.wait_ge(c_by_act, u + 2)
                if banks is not last_banks:
                    pe.wait_ge(banks_free, u + 1)
                for n in range(K_TILES):
                    last = pe.transpose(banks[n // 2][:, n % 2, :], C[:, n * P:(n + 1) * P], ident[:, :])
                last.then_inc(c_turned, 1)

            def layer1(u, m, banks=banks):
                if m >= 2:
                    pe.wait_ge(h1_ready, M1 * u + m - 1)
                for k in range(K_TILES):
                    if m == 0 and k == 0:
                        pe.wait_ge(tt_by_dve, u + 1)
                    if m == 0 and k == K_TILES // 2:
                        pe.wait_ge(tt_by_act, u + 1)
                    last = pe.matmul(banks[m % 2][:, m, :], w1_sb[:, k, m * P:(m + 1) * P], TT[:, k, :],
                                     start=(k == 0), stop=(k == K_TILES - 1))
                last.then_inc(h1_summed, 1)

            def layer2(u, banks=banks):
                for m in range(M2):
                    for k in range(M1):
                        if m == 0 and k == 0:
                            pe.wait_ge(h1_ready, M1 * u + M1 - 1)
                        if m == 0 and k == M1 - 1:
                            pe.wait_ge(h1_ready, M1 * (u + 1))
                        last = pe.matmul(banks[m % 2][:, m, :], w2_sb[:, k, m * P:(m + 1) * P], h1[:, k, :],
                                         start=(k == 0), stop=(k == M1 - 1))
                    last.then_inc(h2_summed, 1)

            def layer3(u, banks=banks):
                pe.wait_ge(h2_ready, M2 * (u + 1))
                for k in range(M2):
                    last = pe.matmul(banks[0][0:1, 3, :], w3_sb[:, k:k + 1], h2[:, k, :],
                                     start=(k == 0), stop=(k == M2 - 1))
                last.then_inc(y_summed, 1)

            def tile_step(t, k, dots=True, layered=True):
                for pair in range(PAIRS):
                    turn_pair(t, pair, not dots)
                    if layered:
                        if pair == 2:
                            turn_c(t - 2)
                        if pair in LAYER1_AFTER:
                            layer1(t - 2, LAYER1_AFTER[pair])
                        if pair == LAYER2_AFTER[k]:
                            layer2(t - 2)
                        if pair == LAYER3_AFTER[k]:
                            layer3(t - 2)
                    for g in dots_after(k, pair, dots, layered):
                        dots_group(t - 1, 1 - k, g, not layered)
                    q = chunk_after(k, pair, dots, layered)
                    if q is not None:
                        look_up(t + k, q, not dots)

            def last_step(t, k):
                for pair in range(PAIRS):
                    turn_pair(t, pair)
                    if pair < GROUPS:
                        dots_group(t - 1, 1 - k, pair)
                    if pair == 3:
                        turn_c(t - 2)
                    if 4 <= pair < 8:
                        layer1(t - 2, pair - 4)
                    if pair == 9:
                        layer2(t - 2)
                    if pair == 10:
                        layer3(t - 2)
                turn_c(t - 1)
                for g in range(GROUPS):
                    dots_group(t, k, g)
                    if g in (3, 7):
                        layer1(t - 1, g // 4)
                layer1(t - 1, 2)
                layer1(t - 1, 3)
                layer2(t - 1)
                pe.wait_ge(c_by_dve, 1)
                turn_c(t, last_banks)
                for m in range(M1):
                    layer1(t, m, last_banks)
                    if m == 1:
                        layer3(t - 1)
                layer2(t, last_banks)
                layer3(t, last_banks)

            pe.sem_inc(c_turned, 1)
            for q in (0, 1):
                look_up(0, q, first=True)
            pe.wait_ge(ident_ready, 1)
            tile_step(0, 0, dots=False, layered=False)
            tile_step(1, 1, layered=False)
            pe.wait_ge(w1_landed, 16)
            pe.wait_ge(w2_landed, 16)
            pe.wait_ge(small_landed, 48)
            with pe.Fori(1, TILES // 2 - 1) as i:
                tile_step(2 * i, 0)
                tile_step(2 * i + 1, 1)
            tile_step(TILES - 2, 0)
            last_step(TILES - 1, 1)

        def copy_dots(engine_copy, g, j):
            lanes = slice(32 * j, 32 * j + 32)
            src = dots_ps[g % 2][lanes, :, 32 * j:32 * j + 32]
            dst = Z[lanes, :, g * GROUP:(g + 1) * GROUP].rearrange("p m q -> p q m")
            return engine_copy(dst, src)

        def copy_turned(engine_copy, k, pair):
            f0, f1 = GATHERED[2 * pair:2 * pair + 2]
            dst = XT[k][:, :, :, f0:f1 + 1:f1 - f0].rearrange("p h b e -> p e h b")
            return engine_copy(dst, xt_ps[pair % 2][:, :, :, :])

        def pick_parts(engine_copy, first, last):
            sizes = [(m1 - m0) * (i1 - i0) for m0, m1, i0, i1 in PARTS]
            for n in range(first, last):
                m0, m1, i0, i1 = PARTS[n]
                at = sum(sizes[:n])
                dst = C[:, at:at + sizes[n]].rearrange("p (m i) -> p m i", i=i1 - i0)
                done = engine_copy(dst, T[:, m0:m1, i0:i1])
            return done

        @block.vector
        def _(dve):
            def copy(dst, src):
                return dve.tensor_copy(dst, src)

            def even_pair(t, k, pair, early=False):
                dve.wait_ge(turned, PAIRS * t + pair + 1)
                if pair == 0 and not early:
                    dve.wait_ge(dots_done, GROUPS * (t - 1))
                copy_turned(copy, k, pair).then_inc(xt_by_dve, 1)

            def dots_group(u, g, first=False):
                dve.wait_ge(dots_done, GROUPS * u + g + 1)
                if g == 0 and not first:
                    dve.wait_ge(z_turned, u)
                copy_dots(copy, g, 0)
                copy_dots(copy, g, 1).then_inc(z_by_dve, 1)

            def turn_z(u):
                dve.wait_ge(z_by_dve, GROUPS * (u + 1))
                dve.wait_ge(z_by_act, GROUPS * (u + 1))
                dve.wait_ge(c_by_act, u + 1)
                dve.transpose(T[:, :, :], Z[:, :, :]).then_inc(z_turned, 1)
                dve.wait_ge(z_turned, u + 1)
                dve.sem_inc(t_waited, 1)
                for n in range(N_SQUARES):
                    before, square = ([T[:, m:m + B, m:m + B] for m in (16 * n, 16 * n + B)])
                    done = dve.copy_predicated(square, below[:, n].bitcast(U32), before)
                done.then_inc(squares_set, 1)
                dve.wait_ge(squares_set, u + 1)
                dve.sem_inc(t_waited, 1)
                for n in range(N_SQUARES):
                    at = (16 * n + B) * (N_FEAT + 1)
                    diagonal = T[:, :, :].rearrange("p m i -> p (m i)")[:, at:at + B * (N_FEAT + 1) - N_FEAT:N_FEAT + 1]
                    done = dve.tensor_copy(diagonal, dense_sb[:, u, B * n:B * n + B])
                done.then_inc(t_ready, 1)

            def operand(u, banks=banks):
                dve.wait_ge(c_turned, u + 2)
                dve.tensor_copy(TT[:, 0:2, :], banks[0][:, 0:2, :]).then_inc(tt_by_dve, 1)

            def make_onehot(t, q, first=False):
                n, c = q // 2, q % 2
                if q == 0:
                    dve.wait_ge(ids_all_landed, 8 * t + 16)
                if not (first and q < 2):
                    dve.wait_ge(looked_up, N_LOOK * t + q - 1)
                rows = row_of[:, HALF_ROWS * c:HALF_ROWS * (c + 1)].rearrange("p (r o) -> p r o", o=1)
                dve.tensor_tensor(onehot[c][:, :, :], ids_all[:, n:n + 1, :].broadcast_to([P, HALF_ROWS, 2 * P]),
                                  rows.broadcast_to([P, HALF_ROWS, 2 * P]), ALU.is_equal).then_inc(onehot_ready, 1)

            def move_looked(t):
                dve.wait_ge(looked_by_act, N_LOOK // 2 * (t + 1))
                for n in range(0, N_LOOK, 2):
                    f0, f1 = LOOKED[n:n + 2]
                    dst = XT[1][:, :, :, f0:f1 + 1:f1 - f0].rearrange("p h b e -> p e h b")
                    dve.tensor_copy(dst, looked_next[:, n:n + 2, :, :]).then_inc(looked_moved, 1)

            def tile_step(t, k, dots=True, layered=True):
                for pair in range(PAIRS):
                    if pair % 2 == 0:
                        even_pair(t, k, pair, not layered)
                    if layered and pair == 2:
                        operand(t - 2)
                    if dots and pair == 12:
                        turn_z(t - 1)
                    for g in dots_after(k, pair, dots, layered):
                        dots_group(t - 1, g, not layered)
                    if k == 1 and pair == 2:
                        move_looked(t)
                    onehot_after = (4, 6) if layered else (2, 3)
                    if k == 1 and pair in onehot_after:
                        make_onehot(t + 1, onehot_after.index(pair))
                    q = chunk_after(k, pair, dots, layered)
                    if q is not None and q + 2 < CHUNKS:
                        make_onehot(t + k, q + 2)

            def last_step(t, k):
                for pair in range(0, PAIRS, 2):
                    even_pair(t, k, pair)
                    if pair == 2:
                        move_looked(t)
                    if pair == 4:
                        operand(t - 2)
                    for g in (pair, pair + 1):
                        if g < GROUPS:
                            dots_group(t - 1, g)
                    if pair == 8:
                        turn_z(t - 1)
                operand(t - 1)
                for g in range(GROUPS):
                    dots_group(t, g)
                turn_z(t)
                dve.wait_ge(t_ready, t + 1)
                pick_parts(copy, len(PARTS) - N_SQUARES, len(PARTS)).then_inc(c_by_dve, 1)
                operand(t, last_banks)

            for n in range(N_LOOK):
                dve.wait_ge(hi_ready, n + 1)
                dve.tensor_tensor(table_lo[n][0:ROWS], stage[n][0:ROWS], table_hi[n][0:ROWS].bitcast(F32),
                                  ALU.subtract).then_inc(lo_ready, 1)
                if n == 0:
                    dve.wait_ge(row_of_ready, 1)
                    make_onehot(0, 0, first=True)
                    make_onehot(0, 1, first=True)
                if 0 < n < 3:
                    make_onehot(0, n + 1, first=True)
            tile_step(0, 0, dots=False, layered=False)
            dve.wait_ge(lo_ready, N_LOOK)
            dve.wait_ge(below_ready, 2)
            dve.wait_ge(dense_landed, 64)
            tile_step(1, 1, layered=False)
            with dve.Fori(1, TILES // 2 - 1) as i:
                tile_step(2 * i, 0)
                tile_step(2 * i + 1, 1)
            tile_step(TILES - 2, 0)
            last_step(TILES - 1, 1)

        @block.scalar
        def _(act):
            def copy(dst, src):
                return act.activation(dst, src, ACT.Copy)

            def odd_pair(t, k, pair, early=False):
                act.wait_ge(turned, PAIRS * t + pair + 1)
                if pair == 1 and not early:
                    act.wait_ge(dots_done, GROUPS * (t - 1))
                copy_turned(copy, k, pair).then_inc(xt_by_act, 1)

            def dots_group(u, g, first=False):
                act.wait_ge(dots_done, GROUPS * u + g + 1)
                if g == 0 and not first:
                    act.wait_ge(z_turned, u)
                copy_dots(copy, g, 2)
                copy_dots(copy, g, 3).then_inc(z_by_act, 1)

            def pick(u, squares=True):
                act.wait_ge(z_turned, u + 1)
                act.wait_ge(c_turned, u + 1)
                done = pick_parts(copy, 0, len(PARTS) - N_SQUARES)
                if squares:
                    act.wait_ge(t_ready, u + 1)
                    done = pick_parts(copy, len(PARTS) - N_SQUARES, len(PARTS))
                done.then_inc(c_by_act, 1)

            def operand(u, banks=banks):
                act.wait_ge(c_turned, u + 2)
                copy(TT[:, 2:4, :], banks[1][:, 0:2, :]).then_inc(tt_by_act, 1)

            def relu1(u, m, banks=banks):
                act.wait_ge(h1_summed, M1 * u + m + 1)
                act.activation(h1[:, m, :], banks[m % 2][:, m, :], ACT.Relu, bias=b1_sb[:, m:m + 1]).then_inc(h1_ready, 1)

            def relu2(u, banks=banks):
                for m in range(M2):
                    act.wait_ge(h2_summed, M2 * u + m + 1)
                    act.activation(h2[:, m, :], banks[m % 2][:, m, :], ACT.Relu, bias=b2_sb[:, m:m + 1]).then_inc(h2_ready, 1)

            def out(u, banks=banks):
                act.wait_ge(y_summed, u + 1)
                act.wait_ge(y_stored, 16 * (u + 1))
                copy(y_q, banks[0][0:1, 3, :].rearrange("o (j q) -> o j q", j=4)).then_inc(banks_free, 1)

            def store_looked(t, n, first=False):
                act.wait_ge(looked_up, N_LOOK * t + 2 * n + 2)
                if n == 0 and not first:
                    act.wait_ge(looked_moved, t)
                for h in range(HALVES):
                    copy(XT[0][:, h, :, LOOKED[n]], look_ps[h][:, 0, 0:P])
                    done = copy(looked_next[:, n, h, :], look_ps[h][:, 0, P:2 * P])
                done.then_inc(looked_by_act, 1)

            def tile_step(t, k, dots=True, layered=True):
                for pair in range(PAIRS):
                    if pair % 2 == 1:
                        odd_pair(t, k, pair, not layered)
                    if layered:
                        if pair == 1:
                            pick(t - 2)
                        if pair == 2:
                            operand(t - 2)
                        if pair in LAYER1_AFTER:
                            relu1(t - 2, LAYER1_AFTER[pair])
                        if pair == LAYER2_AFTER[k]:
                            relu2(t - 2)
                        if pair == LAYER3_AFTER[k]:
                            out(t - 2)
                    for g in dots_after(k, pair, dots, layered):
                        dots_group(t - 1, g, not layered)
                    q = chunk_after(k, pair, dots, layered)
                    if q is not None and q % 2 == 1:
                        store_looked(t + k, q // 2, not dots)

            def last_step(t, k):
                for pair in range(PAIRS):
                    if pair % 2 == 1:
                        odd_pair(t, k, pair)
                    if pair == 1:
                        pick(t - 2)
                    if pair < GROUPS:
                        dots_group(t - 1, pair)
                    if pair == 3:
                        operand(t - 2)
                    if 4 <= pair < 8:
                        relu1(t - 2, pair - 4)
                    if pair == 9:
                        relu2(t - 2)
                        pick(t - 1)
                    if pair == 10:
                        out(t - 2)
                operand(t - 1)
                for g in range(GROUPS):
                    dots_group(t, g)
                    if g in (3, 7):
                        relu1(t - 1, g // 4)
                relu1(t - 1, 2)
                relu1(t - 1, 3)
                pick(t, squares=False)
                operand(t, last_banks)
                relu2(t - 1)
                for m in range(M1):
                    relu1(t, m, last_banks)
                    if m == 1:
                        out(t - 1)
                relu2(t, last_banks)
                out(t, last_banks)

            act.sem_inc(banks_free, 1)
            act.sem_inc(c_by_act, 1)
            for n in range(N_LOOK):
                act.wait_ge(tables_landed[n], 16)
                copy(table_hi[n][0:ROWS], stage[n][0:ROWS]).then_inc(hi_ready, 1)
            store_looked(0, 0, first=True)
            tile_step(0, 0, dots=False, layered=False)
            act.wait_ge(lo_ready, N_LOOK)
            tile_step(1, 1, layered=False)
            act.wait_ge(small_landed, 48)
            with act.Fori(1, TILES // 2 - 1) as i:
                tile_step(2 * i, 0)
                tile_step(2 * i + 1, 1)
            tile_step(TILES - 2, 0)
            last_step(TILES - 1, 1)


def kernel(**inputs):
    import numpy as np
    import concourse.bacc as bacc
    from concourse.bass_utils import run_bass_kernel_spmd

    nc = bacc.Bacc("TRN2", target_bir_lowering=False, num_devices=1)
    arrays = {}

    def given(name, a):
        a = np.ascontiguousarray(a)
        arrays[name] = a
        return nc.dram_tensor(name, a.shape, mybir.dt.from_np(a.dtype), kind="ExternalInput").ap()

    w_top1 = np.asarray(inputs["W_top1"])
    w1 = w_top1[operand_rows()]

    ids = given("ids", inputs["ids"])
    ids_looked = given("ids_looked", np.asarray(inputs["ids"])[:, list(LOOKED)].T)
    dense = given("dense_ctx", inputs["dense_ctx"])
    tables = [given(f"tbl_{f}", inputs[f"tbl_{f}"]) for f in range(N_FEAT)]
    w1 = given("w1", w1.reshape(K_TILES, P, -1))
    b1 = given("b1", np.asarray(inputs["b_top1"]).reshape(-1, P).T)
    w2 = given("w2", inputs["W_top2"])
    b2 = given("b2", np.asarray(inputs["b_top2"]).reshape(-1, P).T)
    w3 = given("w3", np.asarray(inputs["W_top3"]).reshape(-1, P).T)
    y = nc.dram_tensor("y", (dense.shape[0], 1), F32, kind="ExternalOutput").ap()
    build(nc, ids, ids_looked, dense, tables, w1, b1, w2, b2, w3, y)
    result = run_bass_kernel_spmd(nc, [arrays], core_ids=[0])
    return result.results[0]["y"]
```
